# Optimizing a Trainium2 kernel written in Bass

```python
import numpy as np
import jax
import jax.numpy as jnp

def _softmax(x, axis=-1):
    return jax.nn.softmax(x, axis=axis)

def _gelu(x):
    return jax.nn.gelu(x, approximate=True)

def _silu(x):
    return jax.nn.silu(x)

def _sigmoid(x):
    return jax.nn.sigmoid(x)

def _layernorm(x, axis=-1, eps=1e-05):
    m = jnp.mean(x, axis=axis, keepdims=True)
    v = jnp.var(x, axis=axis, keepdims=True)
    return (x - m) / jnp.sqrt(v + eps)

def _scatter_add(tgt, idx, src, axis=0):
    return tgt.at[idx].add(src)

def _segment_sum(src, seg, n):
    return jax.ops.segment_sum(src, seg, n)
kernel_name = 'mk_xattn_ffn_d2_seqx_r8_bf7884'

def setup_inputs(seed: int=0):
    np.random.seed(seed)
    _w = jnp.asarray

    def _rec_inputs():
        import jax
        import jax.numpy as jnp
        _rk = jax.random.key(seed)
        x = 7.22e-05 + 1 * jax.random.normal(jax.random.fold_in(_rk, 1), (128, 64, 128), jnp.float32)
        _lenS = 64 - jax.random.randint(jax.random.fold_in(_rk, 7), (128,), 0, max(1, 64 // 4) + 1, jnp.int32)
        _lenS2 = 64 - jax.random.randint(jax.random.fold_in(_rk, 8), (128,), 0, max(1, 64 // 4) + 1, jnp.int32)
        _ctx_1024P = jax.random.normal(jax.random.fold_in(_rk, 11), (128, 16, 128), jnp.float32)
        _ctx_1024c = jax.random.dirichlet(jax.random.fold_in(_rk, 511), 0.3 * jnp.ones((16,), jnp.float32), (128, 64))
        _ctx_1024t = jnp.einsum('bsk,bkd->bsd', _ctx_1024c, _ctx_1024P)
        _ctx_1024t = _ctx_1024t * jax.lax.rsqrt(jnp.mean(jnp.square(_ctx_1024t)) + 1e-12) * 0.953939
        ctx_1024 = 4.13588e-05 + 0.999923 * (_ctx_1024t + 0.3 * jax.random.normal(jax.random.fold_in(_rk, 611), (128, 64, 128), jnp.float32))
        _validS = jnp.arange(64)[None, :] < _lenS[:, None]
        _validS2 = jnp.arange(64)[None, :] < _lenS2[:, None]
        _causal = jnp.tril(jnp.ones((64, 64), dtype=bool))
        mask_BxS2_ik0 = jnp.where(jnp.broadcast_to(_validS2[:, :], (128, 64)), 0, 1).astype(jnp.int32)
        mask_BxSxS2_bf1 = jnp.ones((128, 64, 64), dtype=bool)
        return (x, ctx_1024, mask_BxS2_ik0, mask_BxSxS2_bf1)
    x, ctx_1024, mask_BxS2_ik0, mask_BxSxS2_bf1 = _rec_inputs()

    def _L0_xattn_setup():
        import jax, jax.numpy as jnp
        import numpy as np
        import math
        B, S, HID, H = (4, 256, 128, 16)
        D = HID // H
        key = jax.random.key(seed)
        ks = jax.random.split(key, 13)
        xavier = lambda k: jax.random.normal(k, (HID, HID), jnp.float32) * math.sqrt(2.0 / (HID + HID))
        return {'q': jax.random.normal(ks[0], (B, S, HID), jnp.float32), 'k': jax.random.normal(ks[1], (B, S, HID), jnp.float32), 'v': jax.random.normal(ks[2], (B, S, HID), jnp.float32), 'padding_mask': jax.random.randint(ks[3], (B, S), 0, 2, jnp.int32), 'Wq': xavier(ks[4]), 'bq': jnp.zeros((HID,), jnp.float32), 'Wk': xavier(ks[5]), 'bk': jnp.zeros((HID,), jnp.float32), 'Wv': xavier(ks[6]), 'bv': jnp.zeros((HID,), jnp.float32), 'Wo': xavier(ks[7]), 'bo': jnp.zeros((HID,), jnp.float32), 'is_causal': 1}
    _L0_xattn_all = _L0_xattn_setup()
    _L0_xattn_in = {k: v for k, v in _L0_xattn_all.items() if k in ('Wq', 'bq', 'Wk', 'bk', 'Wv', 'bv', 'Wo', 'bo')}
    del _L0_xattn_all

    def _L0_ffn_setup():
        import jax, jax.numpy as jnp
        import numpy as np
        B, S, D, E, H = (2, 128, 128, 16, 256)
        TOP_K = 2
        TEMP = 1.0
        key = jax.random.key(seed)
        ks = jax.random.split(key, 4)
        sc_d = 1.0 / np.sqrt(D)
        sc_h = 1.0 / np.sqrt(H)
        return {'x': jax.random.normal(ks[0], (B, S, D), dtype=jnp.float32), 'Wr': jax.random.normal(ks[1], (D, E), dtype=jnp.float32) * sc_d, 'br': jnp.zeros((E,), dtype=jnp.float32), 'W1': jax.random.normal(ks[2], (E, D, H), dtype=jnp.float32) * sc_d, 'b1': jnp.zeros((E, H), dtype=jnp.float32), 'W2': jax.random.normal(ks[3], (E, H, D), dtype=jnp.float32) * sc_h, 'b2': jnp.zeros((E, D), dtype=jnp.float32)}
    _L0_ffn_all = _L0_ffn_setup()
    _L0_ffn_in = {k: v for k, v in _L0_ffn_all.items() if k in ('Wr', 'br', 'W1', 'b1', 'W2', 'b2')}
    del _L0_ffn_all

    def _L1_xattn_setup():
        import jax, jax.numpy as jnp
        import numpy as np
        DIM = 128
        HEAD_DIM = 64
        NUM_HEADS = DIM // HEAD_DIM
        SCALE = HEAD_DIM ** (-0.5)
        key = jax.random.key(seed)
        k_x, k_ctx, k_wq, k_wkv, k_wo = jax.random.split(key, 5)
        B, N, M = (2, 256, 256)
        x = jax.random.normal(k_x, (B, N, DIM), dtype=jnp.float32)
        context = jax.random.normal(k_ctx, (B, M, DIM), dtype=jnp.float32)
        mask = jnp.ones((B, N, M), dtype=bool)
        s = DIM ** (-0.5)
        Wq = jax.random.normal(k_wq, (DIM, DIM), dtype=jnp.float32) * s
        Wkv = jax.random.normal(k_wkv, (DIM, 2 * DIM), dtype=jnp.float32) * s
        Wo = jax.random.normal(k_wo, (DIM, DIM), dtype=jnp.float32) * s
        return {'x': x, 'context': context, 'mask': mask, 'Wq': Wq, 'Wkv': Wkv, 'Wo': Wo}
    _L1_xattn_all = _L1_xattn_setup()
    _L1_xattn_in = {k: v for k, v in _L1_xattn_all.items() if k in ('Wq', 'Wkv', 'Wo')}
    del _L1_xattn_all

    def _L1_ffn_setup():
        import jax, jax.numpy as jnp
        import numpy as np
        B, T, C, H, E = (1, 32, 128, 256, 8)
        STD = 0.02
        key = jax.random.key(seed)
        ks = jax.random.split(key, 8)
        f32 = jnp.float32
        return {'x': jax.random.normal(ks[0], (B, T, C), f32), 'up': jax.random.normal(ks[1], (E, H, C), f32) * STD, 'gate': jax.random.normal(ks[2], (E, H, C), f32) * STD, 'down': jax.random.normal(ks[3], (E, C, H), f32) * STD, 'router': jax.random.normal(ks[4], (E, C), f32) * STD, 'w_up_s': jax.random.normal(ks[5], (H, C), f32) * STD, 'w_gate_s': jax.random.normal(ks[6], (H, C), f32) * STD, 'w_down_s': jax.random.normal(ks[7], (C, H), f32) * STD}
    _L1_ffn_all = _L1_ffn_setup()
    _L1_ffn_in = {k: v for k, v in _L1_ffn_all.items() if k in ('up', 'gate', 'down', 'router', 'w_up_s', 'w_gate_s', 'w_down_s')}
    del _L1_ffn_all
    return {'x': x, 'ctx_1024': ctx_1024, 'mask_BxS2_ik0': mask_BxS2_ik0, 'mask_BxSxS2_bf1': mask_BxSxS2_bf1, 'L0_xattn_Wq': _L0_xattn_in['Wq'], 'L0_xattn_bq': _L0_xattn_in['bq'], 'L0_xattn_Wk': _L0_xattn_in['Wk'], 'L0_xattn_bk': _L0_xattn_in['bk'], 'L0_xattn_Wv': _L0_xattn_in['Wv'], 'L0_xattn_bv': _L0_xattn_in['bv'], 'L0_xattn_Wo': _L0_xattn_in['Wo'], 'L0_xattn_bo': _L0_xattn_in['bo'], 'L0_ffn_Wr': _L0_ffn_in['Wr'], 'L0_ffn_br': _L0_ffn_in['br'], 'L0_ffn_W1': _L0_ffn_in['W1'], 'L0_ffn_b1': _L0_ffn_in['b1'], 'L0_ffn_W2': _L0_ffn_in['W2'], 'L0_ffn_b2': _L0_ffn_in['b2'], 'L1_xattn_Wq': _L1_xattn_in['Wq'], 'L1_xattn_Wkv': _L1_xattn_in['Wkv'], 'L1_xattn_Wo': _L1_xattn_in['Wo'], 'L1_ffn_up': _L1_ffn_in['up'], 'L1_ffn_gate': _L1_ffn_in['gate'], 'L1_ffn_down': _L1_ffn_in['down'], 'L1_ffn_router': _L1_ffn_in['router'], 'L1_ffn_w_up_s': _L1_ffn_in['w_up_s'], 'L1_ffn_w_gate_s': _L1_ffn_in['w_gate_s'], 'L1_ffn_w_down_s': _L1_ffn_in['w_down_s']}

def reference(x, ctx_1024, mask_BxS2_ik0, mask_BxSxS2_bf1, L0_xattn_Wq, L0_xattn_bq, L0_xattn_Wk, L0_xattn_bk, L0_xattn_Wv, L0_xattn_bv, L0_xattn_Wo, L0_xattn_bo, L0_ffn_Wr, L0_ffn_br, L0_ffn_W1, L0_ffn_b1, L0_ffn_W2, L0_ffn_b2, L1_xattn_Wq, L1_xattn_Wkv, L1_xattn_Wo, L1_ffn_up, L1_ffn_gate, L1_ffn_down, L1_ffn_router, L1_ffn_w_up_s, L1_ffn_w_gate_s, L1_ffn_w_down_s):
    import jax
    import jax.numpy as jnp

    def _L0_xattn_ref(q, k, v, padding_mask, Wq, bq, Wk, bk, Wv, bv, Wo, bo, is_causal):
        import jax, jax.numpy as jnp
        import numpy as np
        import math
        B, S, HID, H = (4, 256, 128, 16)
        D = HID // H
        b, s, _ = q.shape
        proj = lambda x, W, bias: (x @ W.T + bias).reshape(b, s, H, D).transpose(0, 2, 1, 3)
        qh, kh, vh = (proj(q, Wq, bq), proj(k, Wk, bk), proj(v, Wv, bv))
        corr = jnp.einsum('bhqd,bhkd->bhqk', qh, kh) / math.sqrt(D)
        corr = jnp.where(padding_mask[:, None, :, None] == 0, jnp.float32(-1000000000.0), corr)
        if is_causal:
            tri = jnp.triu(jnp.ones((s, s), bool), k=1)
            corr = jnp.where(tri[None, None], -jnp.inf, corr)
        prob = jax.nn.softmax(corr, axis=-1)
        hidden = jnp.einsum('bhqk,bhkd->bhqd', prob, vh)
        hidden = hidden.transpose(0, 2, 1, 3).reshape(b, s, H * D)
        return hidden @ Wo.T + bo

    def _L0_ffn_ref(x, Wr, br, W1, b1, W2, b2):
        import jax, jax.numpy as jnp
        import numpy as np
        B, S, D, E, H = (2, 128, 128, 16, 256)
        TOP_K = 2
        TEMP = 1.0
        token_shape = x.shape[:-1]
        d = x.shape[-1]
        xt = x.reshape(-1, d)
        T = xt.shape[0]
        logits = (xt @ Wr + br) / TEMP
        probs = jax.nn.softmax(logits, axis=-1)
        w, idx = jax.lax.top_k(probs, TOP_K)
        w = w / jnp.clip(jnp.sum(w, axis=-1, keepdims=True), 1e-09)
        comb = jnp.zeros((T, E), dtype=xt.dtype)
        comb = comb.at[jnp.arange(T)[:, None], idx].add(w)
        h = jax.nn.gelu(jnp.einsum('td,edh->teh', xt, W1) + b1, approximate=False)
        o = jnp.einsum('teh,eho->teo', h, W2) + b2
        y = jnp.einsum('teo,te->to', o, comb)
        y = xt + y
        return y.reshape(*token_shape, d)

    def _L1_xattn_ref(x, context, mask, Wq, Wkv, Wo):
        import jax, jax.numpy as jnp
        import numpy as np
        DIM = 128
        HEAD_DIM = 64
        NUM_HEADS = DIM // HEAD_DIM
        SCALE = HEAD_DIM ** (-0.5)
        B, N, C = x.shape
        M = context.shape[1]
        H, D = (NUM_HEADS, HEAD_DIM)
        q = (x @ Wq).reshape(B, N, H, D).transpose(0, 2, 1, 3)
        kv = (context @ Wkv).reshape(B, M, 2, H, D).transpose(2, 0, 3, 1, 4)
        k, v = (kv[0], kv[1])
        attn = jnp.einsum('bhnd,bhmd->bhnm', q, k) * SCALE
        attn = jnp.where(mask[:, None, :, :], attn, -jnp.inf)
        attn = jax.nn.softmax(attn, axis=-1)
        out = jnp.einsum('bhnm,bhmd->bhnd', attn, v)
        out = out.transpose(0, 2, 1, 3).reshape(B, N, C)
        return out @ Wo

    def _L1_ffn_ref(x, up, gate, down, router, w_up_s, w_gate_s, w_down_s):
        import jax, jax.numpy as jnp
        import numpy as np
        B, T, C, H, E = (1, 32, 128, 256, 8)
        STD = 0.02
        b, t, c = x.shape
        x_ = x.reshape(b * t, c)
        logits = x_ @ router.T
        idx = jnp.argmax(logits, axis=-1)
        onehot = jax.nn.one_hot(idx, router.shape[0], dtype=x.dtype)
        u = jnp.einsum('bc,ehc->ebh', x_, up)
        g = jnp.einsum('bc,ehc->ebh', x_, gate)
        h = jax.nn.silu(g) * u
        ye = jnp.einsum('ebh,ech->ebc', h, down)
        y = jnp.einsum('ebc,be->bc', ye, onehot)
        ys = jax.nn.silu(x_ @ w_gate_s.T) * (x_ @ w_up_s.T) @ w_down_s.T
        return (y + ys).reshape(b, t, c)
    x = x + _L0_xattn_ref(_layernorm(x, axis=-1), ctx_1024, ctx_1024, mask_BxS2_ik0, L0_xattn_Wq, L0_xattn_bq, L0_xattn_Wk, L0_xattn_bk, L0_xattn_Wv, L0_xattn_bv, L0_xattn_Wo, L0_xattn_bo, 1)
    x = x + _L0_ffn_ref(_layernorm(x, axis=-1), L0_ffn_Wr, L0_ffn_br, L0_ffn_W1, L0_ffn_b1, L0_ffn_W2, L0_ffn_b2)
    x = x + _L1_xattn_ref(_layernorm(x, axis=-1), ctx_1024, mask_BxSxS2_bf1, L1_xattn_Wq, L1_xattn_Wkv, L1_xattn_Wo)
    x = x + _L1_ffn_ref(_layernorm(x, axis=-1), L1_ffn_up, L1_ffn_gate, L1_ffn_down, L1_ffn_router, L1_ffn_w_up_s, L1_ffn_w_gate_s, L1_ffn_w_down_s)
    return x

_drawn_inputs = setup_inputs


def setup_inputs(seed=0):
    import zlib

    import numpy as np

    out = dict(_drawn_inputs(seed))
    spreads = {'L0_xattn_bq': (0.0, 0.597),
     'L0_xattn_bk': (0.0, 0.8),
     'L0_xattn_bv': (0.0, 0.1),
     'L0_xattn_bo': (0.0, 0.1),
     'L0_ffn_br': (0.0, 0.1),
     'L0_ffn_b1': (0.0, 0.368),
     'L0_ffn_b2': (0.0, 0.1)}
    factors = {'L1_ffn_up': 8.0,
     'L1_ffn_gate': 8.0,
     'L1_ffn_down': 8.0,
     'L1_ffn_router': 8.0,
     'L1_ffn_w_up_s': 8.0,
     'L1_ffn_w_gate_s': 8.0,
     'L1_ffn_w_down_s': 8.0}
    for name, (base, spread) in spreads.items():
        noise = np.random.default_rng([zlib.crc32(name.encode()), seed]).standard_normal(out[name].shape)
        drawn = base * np.exp(spread * noise) if base else spread * noise
        out[name] = jnp.asarray(drawn.astype(out[name].dtype))
    for name, factor in factors.items():
        out[name] = (out[name] * factor).astype(out[name].dtype)
    return out
```

```python
from contextlib import ExitStack

import concourse.bass as bass
from concourse import mybir

F32 = mybir.dt.float32
BF16 = mybir.dt.bfloat16
I32 = mybir.dt.int32
U32 = mybir.dt.uint32
U8 = mybir.dt.uint8
ALU = mybir.AluOpType
ACT = mybir.ActivationFunctionType
AX = mybir.AxisListType

P = 128
B, S, C = 128, 64, 128
TILES = B * S // P
GROUPS = TILES // 2
GT = 2 * P
EPS = 1e-5
BIG = -1e30
H0, D0 = 16, 8
PAIRS = H0 // 2
H1, D1 = 2, 64
E0, E1, FF = 16, 8, 256
HALVES = FF // P


def wait(eng, sem, count):
    if not isinstance(count, int) or count > 0:
        eng.wait_ge(sem, count)


def settle(eng, passed):
    eng.sem_inc(passed, 1)


def within(t, n):
    return not isinstance(t, int) or 0 <= t < n


def rounds(eng, body, n, first=1, last=1, start=0):
    for i in range(start, start + first):
        body(i)
    with eng.Fori(start + first, n - last) as i:
        body(i)
    for i in range(n - last, n):
        body(i)


def opening(nc, A, R):
    CH = 4
    n = TILES // CH
    with ExitStack() as ctx:
        sem = lambda name: R.semaphore(nc, "op_" + name)
        loaded = [sem(f"x{c}") for c in range(CH)]
        made, st_done = sem("made"), sem("st_done")
        block = ctx.enter_context(nc.Block())

        @block.sync
        def _(sp):
            for c in range(CH):
                tiles = slice(c * n, (c + 1) * n)
                sp.dma_start(R.x[:, tiles, :], R.xd[:, tiles, :]).then_inc(loaded[c], 16)

        @block.gpsimd
        def _(pool):
            pool.memset(R.ident[:, :], 0.0).then_inc(made, 1)
            pool.wait_ge(made, 1)
            pool.affine_select(out=R.ident[:, :], in_=R.ident[:, :], compare_op=ALU.not_equal, fill=1.0,
                               base=0, pattern=[[-1, P]], channel_multiplier=1).then_inc(made, 1)
            pool.wait_ge(made, 2)
            pool.tensor_copy(R.ident16[:, :], R.ident[:, :]).then_inc(made, 1)
            pool.wait_ge(made, 3)
            pool.memset(R.eps[:, :], EPS).then_inc(made, 1)

        @block.vector
        def _(dve):
            for c in range(CH):
                dve.wait_ge(loaded[c], 16)
                with dve.Fori(c * n, (c + 1) * n) as t:
                    dve.bn_stats(R.stats[:, t, :], R.x[:, t, :]).then_inc(st_done, 1)


def deviations(nc, R, tag):
    with ExitStack() as ctx:
        sem = lambda name: R.semaphore(nc, f"{tag}_{name}")
        half = ctx.enter_context(nc.sbuf_tensor(tag + "_half", [P, TILES], F32))
        link, var_done, sd_done = sem("link"), sem("var_done"), sem("sd_done")
        block = ctx.enter_context(nc.Block())
        mean = lambda k: R.stats[:, :, 3 * k + 1]
        m2 = lambda k: R.stats[:, :, 3 * k + 2]

        @block.vector
        def _(dve):
            dve.tensor_tensor(R.mean[:, :], mean(0), mean(1), ALU.add).then_inc(link, 1)
            dve.tensor_tensor(half[:, :], mean(0), mean(1), ALU.subtract).then_inc(link, 1)
            dve.tensor_tensor(R.rstd[:, :], m2(0), m2(1), ALU.add).then_inc(link, 1)
            dve.wait_ge(link, 3)
            dve.tensor_scalar(R.mean[:, :], R.mean[:, :], 0.5, None, ALU.mult).then_inc(link, 1)
            dve.tensor_tensor(half[:, :], half[:, :], half[:, :], ALU.mult).then_inc(link, 1)
            dve.tensor_scalar(R.rstd[:, :], R.rstd[:, :], 1.0 / C, None, ALU.mult).then_inc(link, 1)
            dve.wait_ge(link, 6)
            dve.scalar_tensor_tensor(R.rstd[:, :], half[:, :], 0.25, R.rstd[:, :], ALU.mult, ALU.add).then_inc(var_done, 1)
            dve.wait_ge(sd_done, 1)
            dve.reciprocal(R.rstd[:, :], R.rstd[:, :]).then_inc(link, 1)

        @block.scalar
        def _(act):
            act.wait_ge(var_done, 1)
            act.activation(R.rstd[:, :], R.rstd[:, :], ACT.Sqrt, bias=R.eps[:, 0:1]).then_inc(sd_done, 1)


def layer0_attention(nc, A, R):
    NT = TILES
    x_sb, ident, ident16 = R.x, R.ident, R.ident16
    with ExitStack() as ctx:
        sb = lambda name, shape, dt=F32: ctx.enter_context(nc.sbuf_tensor("a0_" + name, shape, dt))
        ps = lambda name, shape: ctx.enter_context(nc.psum_tensor("a0_" + name, shape, F32))
        sem = lambda name: R.semaphore(nc, "a0_" + name)
        w = {n: sb(n, [P, P]) for n in ("wq", "wk", "wv", "wo")}
        bq, bk = sb("bq", [P, 1]), sb("bk", [P, 1])
        bv, bo = sb("bv", [P, S]), sb("bo", [P, C])
        causal = sb("causal", [P, S], BF16)
        ctxT = sb("ctxT", [P, 2, GT])
        pad_i = sb("pad_i", [P, 2, GT], I32)
        pad = sb("pad", [P, 2, GT])
        xn = sb("xn", [P, 2, C])
        xnT = sb("xnT", [P, GT])
        qT, kT = sb("qT", [P, 2, GT]), sb("kT", [P, 2, GT])
        kx = sb("kx", [P, 2, H0, GT])
        vx = sb("vx", [P, 2, 4, PAIRS, 2, D0 + 1])
        mx = sb("mx", [P, 2, H0])
        pr = sb("pr", [P, 2, H0, S])
        prT = sb("prT", [P, 2, PAIRS, P])
        rec = sb("rec", [P, H0])
        ao, aoT = sb("ao", [P, H0, D0]), sb("aoT", [P, P])

        ps_s = ps("ps_s", [P, 2, H0 * S])
        ps_t = ps("ps_t", [P, PAIRS, P])
        ps_p = ps("ps_p", [P, 512])
        ps_o = ps("ps_o", [P, 512])
        o_cols = ps_o[:, 0:H0 * (D0 + 1)].rearrange("p (h c) -> p h c", c=D0 + 1)
        v_ps = ps_p[:, GT:2 * GT].rearrange("p (b j d) -> p b j d", b=4, d=D0)

        w_loaded, consts = sem("w_loaded"), sem("consts")
        loaded = [sem(f"loaded{g}") for g in range(2)]
        passed = sem("passed")
        pad_is0, pad_ready = sem("pad_is0"), sem("pad_ready")
        st_done, xn_ready, xb_done = (sem(n) for n in ("st_done", "xn_ready", "xb_done"))
        xk_done, xnT_ready, kT_ready = sem("xk_done"), sem("xnT_ready"), sem("kT_ready")
        kx_ready = [sem(f"kx_ready{g}") for g in range(2)]
        qv_done, qv_ready = sem("qv_done"), sem("qv_ready")
        s_done, mx_done, d_ready, p_ready = sem("s_done"), sem("mx_done"), sem("d_ready"), sem("p_ready")
        t_done, t_evac, o_done = sem("t_done"), sem("t_evac"), sem("o_done")
        rec_done, ao_ready, aoT_done, aoT_ready = sem("rec_done"), sem("ao_ready"), sem("aoT_done"), sem("aoT_ready")
        y_done, x_done, qv_parts = sem("y_done"), sem("x_done"), sem("qv_parts")
        block = ctx.enter_context(nc.Block())

        @block.sync
        def _(sp):
            def load(G, g):
                wait(sp, pad_ready, G - 1)
                wait(sp, qv_done, G - 1)
                sp.dma_start(ctxT[:, g, :], A["ctxT"][:, bass.ds(GT * G, GT)]).then_inc(loaded[g], 16)
                sp.dma_start(pad_i[:, g, :], A["pad"][:, bass.ds(GT * G, GT)].partition_broadcast(P)).then_inc(loaded[g], 16)

            def spread(G, g):
                wait(sp, kT_ready, G + 1)
                wait(sp, s_done, 2 * G - 2)
                for h in range(H0):
                    rows = slice(h * D0, (h + 1) * D0)
                    sp.dma_start(kx[rows, g, h, :], kT[rows, g, :]).then_inc(kx_ready[g], 16)

            load(0, 0)
            for n in ("wq", "wk", "wv", "wo"):
                sp.dma_start(w[n][:, :], A["a0_" + n]).then_inc(w_loaded, 16)
            sp.dma_start(bq[:, :], A["a0_bq"]).then_inc(w_loaded, 16)
            sp.dma_start(bk[:, :], A["a0_bk"]).then_inc(w_loaded, 16)
            for e in range(2):
                sp.dma_start(bv[e * S:(e + 1) * S, :], A["a0_bv"][e:e + 1, :].partition_broadcast(S)).then_inc(w_loaded, 16)
            sp.dma_start(bo[:, :], A["a0_bo"].partition_broadcast(P)).then_inc(w_loaded, 16)
            load(1, 1)
            sp.wait_ge(consts, 1)
            spread(0, 0)

            def body(i):
                for g in range(2):
                    G = 2 * i + g
                    if within(G + 1, GROUPS):
                        spread(G + 1, 1 - g)
                    if within(G + 2, GROUPS):
                        load(G + 2, g)
            rounds(sp, body, GROUPS // 2)
            for g in range(2):
                sp.wait_ge(kx_ready[g], 16 * H0 * (GROUPS // 2))

        @block.gpsimd
        def _(pool):
            def chained(n, instruction):
                instruction.then_inc(consts, 1)
                pool.wait_ge(consts, n)

            chained(1, pool.memset(kx[:, :, :, :], 0.0))
            chained(2, pool.memset(vx[:, :, :, :, :, :], 0.0))
            for e in range(2):
                chained(3 + e, pool.memset(vx[e * S:(e + 1) * S, :, :, :, e, D0], 1.0))
            chained(5, pool.memset(causal[:, :], 0.0))
            for b in range(2):
                rows = causal[b * S:(b + 1) * S, :]
                chained(6 + b, pool.affine_select(out=rows, in_=rows, compare_op=ALU.is_ge, fill=BIG,
                                                  base=0, pattern=[[-1, S]], channel_multiplier=1))

            def body(i):
                for g in range(2):
                    G = 2 * i + g
                    wait(pool, loaded[g], 32 * (i + 1))
                    wait(pool, pad_ready, G)
                    wait(pool, qv_ready, G - 1)
                    settle(pool, passed)
                    pool.tensor_scalar(pad[:, g, :], pad_i[:, g, :], 0, -1, ALU.is_equal, ALU.mult).then_inc(pad_is0, 1)
                    wait(pool, pad_is0, G + 1)
                    settle(pool, passed)
                    pool.tensor_scalar(pad[:, g, :], pad[:, g, :], 1, None, ALU.add).then_inc(pad_ready, 1)
            rounds(pool, body, GROUPS // 2)

        @block.vector
        def _(dve):
            def norm(G):
                wait(dve, xk_done, G)
                for u in range(2):
                    dve.tensor_scalar(xn[:, u, :], x_sb[:, 2 * G + u, :], R.mean[:, bass.ds(2 * G + u, 1)], R.rstd[:, bass.ds(2 * G + u, 1)],
                                      ALU.subtract, ALU.mult).then_inc(xn_ready, 1)
                wait(dve, xn_ready, 2 * G + 2)
                dve.tensor_tensor(x_sb[:, bass.ds(2 * G, 2), :], x_sb[:, bass.ds(2 * G, 2), :],
                                  bo[:, :].rearrange("p (a c) -> p a c", a=1).broadcast_to([P, 2, C]), ALU.add).then_inc(xb_done, 1)

            def qv(G, g):
                wait(dve, pad_ready, G + 1)
                wait(dve, qv_done, G + 1)
                dve.scalar_tensor_tensor(qT[:, g, :], ps_p[:, 0:GT], bq[:, 0:1], pad[:, g, :],
                                         ALU.add, ALU.mult).then_inc(qv_parts, 1)
                for e in range(2):
                    rows = slice(e * S, (e + 1) * S)
                    bias = bv[rows, :].rearrange("p (b j d) -> p b j d", b=1, d=D0).broadcast_to([S, 4, PAIRS, D0])
                    last = dve.tensor_tensor(vx[rows, g, :, :, e, 0:D0], v_ps[rows], bias, ALU.add)
                last.then_inc(qv_ready, 1)

            dve.wait_ge(w_loaded, 16 * 9)
            dve.wait_ge(consts, 7)
            norm(0)
            norm(1)
            qv(0, 0)

            def body(i):
                for k in range(4):
                    T, par, g = 4 * i + k, k % 2, k // 2
                    if within(T, NT):
                        wait(dve, s_done, T + 1)
                        sc = ps_s[:, par, :].rearrange("p (h k) -> p h k", h=H0)
                        dve.tensor_reduce(mx[:, par, :], sc, AX.X, ALU.max).then_inc(mx_done, 1)
                        wait(dve, mx_done, T + 1)
                        wait(dve, t_done, 2 * T - 2)
                        dve.tensor_tensor(pr[:, par, :, :], sc, mx[:, par, :].rearrange("p (h a) -> p h a", a=1)
                                          .broadcast_to([P, H0, S]), ALU.subtract).then_inc(d_ready, 1)
                    if par == 1 and within(2 * i + g + 1, GROUPS):
                        qv(2 * i + g + 1, 1 - g)
                    if within(T - 2, NT):
                        wait(dve, y_done, T - 1)
                        dve.tensor_tensor(x_sb[:, T - 2, :], ps_o[:, 384:512], x_sb[:, T - 2, :], ALU.add).then_inc(x_done, 1)
                        wait(dve, x_done, T - 1)
                        dve.bn_stats(R.stats[:, T - 2, :], x_sb[:, T - 2, :]).then_inc(st_done, 1)
                    if within(T - 1, NT):
                        wait(dve, o_done, T)
                        dve.reciprocal(rec[:, :], o_cols[:, :, D0]).then_inc(rec_done, 1)
                        wait(dve, rec_done, T)
                        dve.tensor_tensor(ao[:, :, :], o_cols[:, :, 0:D0], rec[:, :].rearrange("p (h a) -> p h a", a=1)
                                          .broadcast_to([P, H0, D0]), ALU.mult).then_inc(ao_ready, 1)
                    if par == 0 and within(2 * i + g + 2, GROUPS) and within(T, NT):
                        norm(2 * i + g + 2)
            rounds(dve, body, NT // 4)
            body(NT // 4)

        @block.scalar
        def _(act):
            def xk(G, g, use):
                wait(act, xk_done, G + 1)
                act.activation(xnT[:, :], ps_p[:, 0:GT], ACT.Copy).then_inc(xnT_ready, 1)
                wait(act, kx_ready[g], 256 * use)
                act.activation(kT[:, g, :], ps_p[:, GT:2 * GT], ACT.Identity, bias=bk[:, 0:1]).then_inc(kT_ready, 1)

            act.wait_ge(w_loaded, 16 * 9)
            xk(0, 0, 0)

            def body(i):
                for k in range(4):
                    T, par, g = 4 * i + k, k % 2, k // 2
                    if within(T - 2, NT):
                        wait(act, aoT_done, T - 1)
                        act.activation(aoT[:, :], ps_o[:, 256:384], ACT.Copy).then_inc(aoT_ready, 1)
                    if par == 0 and within(2 * i + g + 1, GROUPS) and within(T, NT):
                        xk(2 * i + g + 1, 1 - g, i + g)
                    if within(T - 1, NT):
                        for half in range(2):
                            js = slice(4 * half, 4 * half + 4)
                            wait(act, t_done, 2 * (T - 1) + half + 1)
                            act.activation(prT[:, 1 - par, js, :], ps_t[:, js, :], ACT.Copy).then_inc(t_evac, 1)
                    if within(T, NT):
                        wait(act, d_ready, T + 1)
                        act.activation(pr[:, par, :, :], pr[:, par, :, :], ACT.Exp, scale=D0 ** -0.5).then_inc(p_ready, 1)
            rounds(act, body, NT // 4)
            body(NT // 4)

        @block.tensor
        def _(pe):
            def proj_xk(G, g, use):
                wait(pe, loaded[g], 32 * (use + 1))
                wait(pe, xn_ready, 2 * G + 2)
                wait(pe, qv_ready, G)
                for u in range(2):
                    pe.transpose(ps_p[:, u * P:(u + 1) * P], xn[:, u, :], ident[:, :])
                pe.matmul(ps_p[:, GT:2 * GT], w["wk"][:, :], ctxT[:, g, :], start=True, stop=True).then_inc(xk_done, 1)

            def proj_qv(G, g, use):
                wait(pe, xnT_ready, G + 1)
                wait(pe, kT_ready, G + 1)
                pe.matmul(ps_p[:, 0:GT], w["wq"][:, :], xnT[:, :], start=True, stop=True)
                for b in range(4):
                    for e in range(2):
                        last = pe.matmul(ps_p[e * S:(e + 1) * S, GT + b * S:GT + (b + 1) * S],
                                         ctxT[:, g, b * S:(b + 1) * S], w["wv"][:, e * S:(e + 1) * S], start=True, stop=True)
                last.then_inc(qv_done, 1)

            pe.wait_ge(w_loaded, 16 * 9)
            pe.wait_ge(consts, 7)
            proj_xk(0, 0, 0)
            proj_qv(0, 0, 0)

            def body(i):
                for k in range(4):
                    T, par, g, u = 4 * i + k, k % 2, k // 2, k % 2
                    if within(T, NT):
                        if u == 0:
                            wait(pe, kx_ready[g], 256 * (i + 1))
                            wait(pe, qv_ready, 2 * i + g + 1)
                        wait(pe, d_ready, T - 1)
                        for half in range(2):
                            cols = slice(512 * half, 512 * half + 512)
                            hidden = causal[:, :].rearrange("p (a k) -> p a k", a=1).broadcast_to([P, H0 // 2, S])
                            pe.matmul(ps_s[:, par, cols], ident16[:, :], hidden, start=True, stop=False)
                            for b in range(2):
                                q = slice(u * P + b * S, u * P + (b + 1) * S)
                                last = pe.matmul(ps_s[b * S:(b + 1) * S, par, cols], qT[:, g, q],
                                                 kx[:, g, 8 * half:8 * half + 8, q], start=False, stop=True)
                        last.then_inc(s_done, 1)
                    if within(T - 2, NT):
                        wait(pe, ao_ready, T - 1)
                        pe.transpose(ps_o[:, 256:384], ao[:, :, :].rearrange("p h d -> p (h d)"), ident[:, :]).then_inc(aoT_done, 1)
                    G = 2 * i + g
                    if within(T, NT) and within(G + 1, GROUPS):
                        (proj_xk if u == 0 else proj_qv)(G + 1, 1 - g, i + g)
                    if within(T - 1, NT):
                        wait(pe, p_ready, T)
                        wait(pe, t_evac, 2 * (T - 1))
                        for half in range(2):
                            for j in range(4 * half, 4 * half + 4):
                                last = pe.transpose(ps_t[:, j, :], pr[:, 1 - par, 2 * j:2 * j + 2, :].rearrange("p h k -> p (h k)"), ident[:, :])
                            last.then_inc(t_done, 1)
                    if within(T - 2, NT):
                        wait(pe, aoT_ready, T - 1)
                        pe.matmul(ps_o[:, 384:512], aoT[:, :], w["wo"][:, :], start=True, stop=True).then_inc(y_done, 1)
                    if within(T - 1, NT):
                        wait(pe, x_done, T - 2 + 1)
                        g1, u1 = (k - 1) % 4 // 2, (k - 1) % 2
                        for half in range(2):
                            wait(pe, t_evac, 2 * (T - 1) + half + 1)
                            for b in range(2):
                                for j in range(4 * half, 4 * half + 4):
                                    rows = slice(b * S, (b + 1) * S)
                                    last = pe.matmul(ps_o[rows, 18 * j:18 * j + 18], prT[:, 1 - par, j, rows],
                                                     vx[:, g1, 2 * u1 + b, j, :, :].rearrange("p e c -> p (e c)"), start=True, stop=True)
                        last.then_inc(o_done, 1)
            rounds(pe, body, NT // 4)
            body(NT // 4)


def layer1_attention(nc, A, R):
    NG = GROUPS
    with ExitStack() as ctx:
        sb = lambda name, shape, dt=F32: ctx.enter_context(nc.sbuf_tensor("a1_" + name, shape, dt))
        ps = lambda name, shape: ctx.enter_context(nc.psum_tensor("a1_" + name, shape, F32))
        sem = lambda name: R.semaphore(nc, "a1_" + name)
        w = {n: sb(n, [P, P]) for n in ("wq", "wk", "wv", "wo")}
        ctxT = sb("ctxT", [P, 2, GT])
        mask = sb("mask", [P, 2, 2, S], U8)
        hide = sb("hide", [P, 2, 2, S])
        xn = sb("xn", [P, 2, C])
        xnT, qT = sb("xnT", [P, GT]), sb("qT", [P, 2, GT])
        kx = sb("kx", [P, 2, H1, GT])
        vx = sb("vx", [P, 2, 4, P + H1])
        mx = sb("mx", [P, 2, H1])
        pr = sb("pr", [P, 2, 2, H1, S])
        prT = sb("prT", [P, 2, P])
        rec = sb("rec", [P, 2, H1])
        ao, aoT = sb("ao", [P, 2, H1, D1]), sb("aoT", [P, GT])
        ps_xk, ps_qv, ps_s, ps_t, ps_o, ps_a, ps_y = (ps(n, [P, 512]) for n in ("xk", "qv", "s", "t", "o", "a", "y"))
        scores = ps_s[:, 0:2 * P].rearrange("p (u h k) -> p u h k", u=2, h=H1)
        out_cols = ps_o[:, 0:2 * (P + H1)].rearrange("p (u c) -> p u c", u=2)

        w_loaded, consts = sem("w_loaded"), sem("consts")
        loaded = [sem(f"loaded{g}") for g in range(2)]
        is0_done, passed, hide_ready = sem("is0_done"), sem("passed"), sem("hide_ready")
        xn_ready, xk_done, xnT_ready, kx_ready = sem("xn_ready"), sem("xk_done"), sem("xnT_ready"), sem("kx_ready")
        qv_done, qT_ready, qv_ready, s_done, h_done, mx_done = (sem(n) for n in ("qv_done", "qT_ready", "qv_ready", "s_done", "h_done", "mx_done"))
        d_ready, p_ready, t_done, prT_ready, o_done = (sem(n) for n in ("d_ready", "p_ready", "t_done", "prT_ready", "o_done"))
        rec_done, ao_ready, aoT_done, aoT_ready, y_done = (sem(n) for n in ("rec_done", "ao_ready", "aoT_done", "aoT_ready", "y_done"))
        x_done, st_done = sem("x_done"), sem("st_done")
        block = ctx.enter_context(nc.Block())

        @block.sync
        def _(sp):
            def load(G, g):
                wait(sp, hide_ready, G - 1)
                wait(sp, qv_done, G - 1)
                sp.dma_start(ctxT[:, g, :], A["ctxT"][:, bass.ds(GT * G, GT)]).then_inc(loaded[g], 16)
                sp.dma_start(mask[:, g, :, :], A["mask"].rearrange("(t p) k -> p t k", p=P)[:, bass.ds(2 * G, 2), :]).then_inc(loaded[g], 16)

            for n in ("wq", "wk", "wv", "wo"):
                sp.dma_start(w[n][:, :], A["a1_" + n]).then_inc(w_loaded, 16)

            def body(i):
                for g in range(2):
                    load(2 * i + g, g)
            rounds(sp, body, NG // 2, last=0)

        @block.gpsimd
        def _(pool):
            pool.memset(kx[:, :, :, :], 0.0).then_inc(consts, 1)
            pool.wait_ge(consts, 1)
            pool.memset(vx[:, :, :, :], 0.0).then_inc(consts, 1)
            pool.wait_ge(consts, 2)
            for h in range(H1):
                pool.memset(vx[h * S:(h + 1) * S, :, :, P + h], 1.0).then_inc(consts, 1)
                pool.wait_ge(consts, 3 + h)

            def body(i):
                for g in range(2):
                    G = 2 * i + g
                    wait(pool, hide_ready, G)
                    wait(pool, loaded[g], 32 * (i + 1))
                    wait(pool, h_done, G - 1)
                    settle(pool, passed)
                    pool.tensor_scalar(hide[:, g, :, :], mask[:, g, :, :], 0.0, -3e38, ALU.is_equal, ALU.mult).then_inc(is0_done, 1)
                    wait(pool, is0_done, G + 1)
                    settle(pool, passed)
                    pool.tensor_scalar(hide[:, g, :, :], hide[:, g, :, :], 10.0, None, ALU.mult).then_inc(hide_ready, 1)
            rounds(pool, body, NG // 2)

        @block.vector
        def _(dve):
            def norm(G):
                wait(dve, xk_done, G)
                for u in range(2):
                    dve.tensor_scalar(xn[:, u, :], R.x[:, 2 * G + u, :], R.mean[:, bass.ds(2 * G + u, 1)], R.rstd[:, bass.ds(2 * G + u, 1)],
                                      ALU.subtract, ALU.mult).then_inc(xn_ready, 1)

            def qv(G, g):
                wait(dve, qv_done, G + 1)
                dve.tensor_copy(qT[:, g, :], ps_qv[:, 0:GT]).then_inc(qT_ready, 1)
                for h in range(H1):
                    rows = slice(h * S, (h + 1) * S)
                    last = dve.tensor_copy(vx[rows, g, :, h * D1:(h + 1) * D1],
                                           ps_qv[rows, GT:2 * GT].rearrange("p (b d) -> p b d", b=4))
                last.then_inc(qv_ready, 1)

            dve.wait_ge(consts, 4)
            norm(0)
            norm(1)
            qv(0, 0)

            def body(i):
                for g in range(2):
                    G = 2 * i + g
                    if within(G, NG):
                        wait(dve, s_done, G + 1)
                        wait(dve, hide_ready, G + 1)
                        wait(dve, t_done, G - 1)
                        for u in range(2):
                            hb = hide[:, g, u, :].rearrange("p (a k) -> p a k", a=1).broadcast_to([P, H1, S])
                            last = dve.tensor_tensor(pr[:, g, u, :, :], scores[:, u], hb, ALU.add)
                        last.then_inc(h_done, 1)
                        wait(dve, h_done, G + 1)
                        dve.tensor_reduce(mx[:, :, :], pr[:, g, :, :, :], AX.X, ALU.max).then_inc(mx_done, 1)
                        wait(dve, mx_done, G + 1)
                        flat = lambda t: t.rearrange("p u h k -> p (u h) k")
                        dve.tensor_tensor(flat(pr[:, g, :, :, :]), flat(pr[:, g, :, :, :]),
                                          mx[:, :, :].rearrange("p u (h a) -> p (u h) a", a=1).broadcast_to([P, 2 * H1, S]), ALU.subtract).then_inc(d_ready, 1)
                    if within(G - 2, NG):
                        wait(dve, y_done, G - 1)
                        t = bass.ds(2 * (G - 2), 2)
                        dve.tensor_tensor(R.x[:, t, :], ps_y[:, 0:GT].rearrange("p (u c) -> p u c", u=2), R.x[:, t, :], ALU.add).then_inc(x_done, 1)
                        wait(dve, x_done, G - 1)
                        for u in range(2):
                            dve.bn_stats(R.stats[:, 2 * (G - 2) + u, :], R.x[:, 2 * (G - 2) + u, :]).then_inc(st_done, 1)
                    if within(G - 1, NG):
                        wait(dve, o_done, G)
                        dve.reciprocal(rec[:, :, :], out_cols[:, :, P:P + H1]).then_inc(rec_done, 1)
                        wait(dve, rec_done, G)
                        for u in range(2):
                            rb = rec[:, u, :].rearrange("p (h a) -> p h a", a=1).broadcast_to([P, H1, D1])
                            last = dve.tensor_tensor(ao[:, u, :, :], out_cols[:, u, 0:P].rearrange("p (h d) -> p h d", h=H1), rb, ALU.mult)
                        last.then_inc(ao_ready, 1)
                    if within(G + 1, NG):
                        qv(G + 1, 1 - g)
                    if within(G + 2, NG):
                        norm(G + 2)
            rounds(dve, body, NG // 2)
            body(NG // 2)

        @block.scalar
        def _(act):
            def xk(G, g):
                wait(act, xk_done, G + 1)
                act.activation(xnT[:, :], ps_xk[:, 0:GT], ACT.Copy).then_inc(xnT_ready, 1)
                wait(act, s_done, G - 1)
                for h in range(H1):
                    rows = slice(h * D1, (h + 1) * D1)
                    last = act.activation(kx[rows, g, h, :], ps_xk[rows, GT:2 * GT], ACT.Copy)
                last.then_inc(kx_ready, 1)

            act.wait_ge(consts, 4)
            xk(0, 0)

            def body(i):
                for g in range(2):
                    G = 2 * i + g
                    if within(G - 2, NG):
                        wait(act, aoT_done, G - 1)
                        act.activation(aoT[:, :], ps_a[:, 0:GT], ACT.Copy).then_inc(aoT_ready, 1)
                    if within(G + 1, NG):
                        xk(G + 1, 1 - g)
                    if within(G - 1, NG):
                        wait(act, t_done, G)
                        act.activation(prT[:, :, :], ps_t[:, 0:GT].rearrange("p (u q) -> p u q", u=2), ACT.Copy).then_inc(prT_ready, 1)
                    if within(G, NG):
                        wait(act, d_ready, G + 1)
                        act.activation(pr[:, g, :, :, :], pr[:, g, :, :, :], ACT.Exp, scale=D1 ** -0.5).then_inc(p_ready, 1)
            rounds(act, body, NG // 2)
            body(NG // 2)

        @block.tensor
        def _(pe):
            def proj_xk(G, g, use):
                wait(pe, loaded[g], 32 * (use + 1))
                wait(pe, xn_ready, 2 * G + 2)
                wait(pe, kx_ready, G)
                for u in range(2):
                    pe.transpose(ps_xk[:, u * P:(u + 1) * P], xn[:, u, :], R.ident[:, :])
                pe.matmul(ps_xk[:, GT:2 * GT], w["wk"][:, :], ctxT[:, g, :], start=True, stop=True).then_inc(xk_done, 1)

            def proj_qv(G, g):
                wait(pe, xnT_ready, G + 1)
                wait(pe, qv_ready, G)
                pe.matmul(ps_qv[:, 0:GT], w["wq"][:, :], xnT[:, :], start=True, stop=True)
                for b in range(4):
                    for h in range(H1):
                        last = pe.matmul(ps_qv[h * S:(h + 1) * S, GT + b * S:GT + (b + 1) * S],
                                         ctxT[:, g, b * S:(b + 1) * S], w["wv"][:, h * S:(h + 1) * S], start=True, stop=True)
                last.then_inc(qv_done, 1)

            pe.wait_ge(w_loaded, 16 * 4)
            pe.wait_ge(consts, 4)
            proj_xk(0, 0, 0)
            proj_qv(0, 0)

            def body(i):
                for g in range(2):
                    G = 2 * i + g
                    if within(G, NG):
                        wait(pe, kx_ready, G + 1)
                        wait(pe, qv_ready, G + 1)
                        wait(pe, h_done, G)
                        for u in range(2):
                            for b in range(2):
                                q = slice(u * P + b * S, u * P + (b + 1) * S)
                                last = pe.matmul(ps_s[b * S:(b + 1) * S, u * P:(u + 1) * P], qT[:, g, q], kx[:, g, :, q], start=True, stop=True)
                        last.then_inc(s_done, 1)
                    if within(G - 2, NG):
                        wait(pe, ao_ready, G - 1)
                        for u in range(2):
                            last = pe.transpose(ps_a[:, u * P:(u + 1) * P], ao[:, u, :, :].rearrange("p h d -> p (h d)"), R.ident[:, :])
                        last.then_inc(aoT_done, 1)
                    if within(G + 1, NG):
                        proj_xk(G + 1, 1 - g, i + g)
                    if within(G - 1, NG):
                        wait(pe, p_ready, G)
                        for u in range(2):
                            last = pe.transpose(ps_t[:, u * P:(u + 1) * P], pr[:, 1 - g, u, :, :].rearrange("p h k -> p (h k)"), R.ident[:, :])
                        last.then_inc(t_done, 1)
                    if within(G - 2, NG):
                        wait(pe, aoT_ready, G - 1)
                        wait(pe, x_done, G - 2)
                        for u in range(2):
                            last = pe.matmul(ps_y[:, u * P:(u + 1) * P], aoT[:, u * P:(u + 1) * P], w["wo"][:, :], start=True, stop=True)
                        last.then_inc(y_done, 1)
                    if within(G - 1, NG):
                        wait(pe, prT_ready, G)
                        wait(pe, ao_ready, G - 1)
                        for u in range(2):
                            for b in range(2):
                                rows = slice(b * S, (b + 1) * S)
                                last = pe.matmul(out_cols[rows, u, :], prT[:, u, rows], vx[:, 1 - g, 2 * u + b, :], start=True, stop=True)
                        last.then_inc(o_done, 1)
                    if within(G + 1, NG):
                        proj_qv(G + 1, 1 - g)
            rounds(pe, body, NG // 2)
            body(NG // 2)


def end_phase(nc, R):
    with nc.Block() as block:
        @block.gpsimd
        def _(pool):
            for s in R.semaphores:
                pool.sem_clear(s)
    for s in R.semaphores:
        nc.release_semaphore(s)
    R.semaphores = []


class Routing:
    REGION = B * S + P

    def __init__(self, nc, ctx, tag, experts, top, width):
        sb = lambda name, shape, dt=F32: ctx.enter_context(nc.sbuf_tensor(f"{tag}_{name}", shape, dt))
        self.tag, self.experts, self.top, self.width = tag, experts, top, width
        self.slots = TILES * top + experts
        self.rows_in = nc.dram_tensor(f"{tag}_rows_in", (experts * self.REGION, C), F32, kind="Internal").ap()
        self.rows_out = nc.dram_tensor(f"{tag}_rows_out", (self.slots * P, C), F32, kind="Internal").ap()
        self.w = sb("w", [P, experts, width])
        self.best = sb("best", [P, TILES, 8])
        self.hit = sb("hit", [P, top, TILES, experts], BF16)
        self.pos = sb("pos", [P, top, TILES])
        self.pos_i = sb("pos_i", [P, top, TILES], I32)
        self.slot_e = sb("slot_e", [P, self.slots], I32)
        self.slot_row = sb("slot_row", [P, self.slots], I32)


def route(nc, A, R, N, add_norm, shared):
    E, K, tag, REGION = N.experts, N.top, N.tag, N.REGION
    WE = A[tag + "_w"].shape[2]
    CT = 16
    CHUNKS, CG = TILES // CT, CT // 2
    with ExitStack() as ctx:
        sb = lambda name, shape, dt=F32: ctx.enter_context(nc.sbuf_tensor(f"{tag}r_{name}", shape, dt))
        ps = lambda name, shape: ctx.enter_context(nc.psum_tensor(f"{tag}r_{name}", shape, F32))
        sem = lambda name: R.semaphore(nc, f"{tag}r_{name}")
        wr = sb("wr", [P, E])
        br = sb("br", [P, E])
        if shared:
            ws = sb("ws", [P, 2 * FF + HALVES * C])
            hg, hT = sb("hg", [P, HALVES, GT]), sb("hT", [P, 2, HALVES, GT])
            ps_u, ps_g, ps_y = ps("ps_u", [P, HALVES, GT]), ps("ps_g", [P, HALVES, GT]), ps("ps_y", [P, 512])
        xn = sb("xn", [P, 2, 2, C])
        xn_all = sb("xn_all", [P, TILES, C])
        xnT = sb("xnT", [P, 2, GT])
        logits = sb("logits", [P, CT, E])
        index = sb("index", [P, CT, 8], U32)
        index_f = sb("index_f", [P, CT, K])
        chosen = sb("chosen", [P, CT, E], BF16)
        earlier, ones = sb("earlier", [P, P], BF16), sb("ones", [P, P], BF16)
        e_i, e_f = sb("e_i", [P, E], I32), sb("e_f", [P, E])
        start, base = sb("start", [P, E]), sb("base", [P, E])
        rank, prod = sb("rank", [P, CT, E]), sb("prod", [P, TILES, E])
        cnt_i, need, ends, ends2 = sb("cnt_i", [P, E], I32), sb("need", [P, E]), sb("ends", [P, E]), sb("ends2", [P, E])
        tail = sb("tail", [P, E], I32)
        shift = sb("shift", [P, E])
        slot_i, slot_f = sb("slot_i", [P, N.slots], I32), sb("slot_f", [P, N.slots])
        by_slot, slot_x = sb("by_slot", [P, N.slots, E]), sb("slot_x", [P, N.slots])
        moved = sb("moved", [P, TILES])
        zeros = sb("zeros", [P, C])
        ps_x, ps_l, ps_r = ps("ps_x", [P, 512]), ps("ps_l", [P, 512]), ps("ps_r", [P, 512])
        rank_ps = ps_r[:, 0:(CT + 1) * E].rearrange("p (t e) -> p t e", e=E)

        w_loaded, ew_loaded, consts, link = sem("w_loaded"), sem("ew_loaded"), sem("consts"), sem("link")
        xn_ready, x_done, xT_done, xT_ready, kept = sem("xn_ready"), sem("x_done"), sem("xT_done"), sem("xT_ready"), sem("kept")
        l_done, l_ready, chosen_ready, ranked, routed = sem("l_done"), sem("l_ready"), sem("chosen_ready"), sem("ranked"), sem("routed")
        sent, table_ready, cleared = sem("sent"), sem("table_ready"), sem("cleared")
        ug_done, g_ready, h_ready, y_done = sem("ug_done"), sem("g_ready"), sem("h_ready"), sem("y_done")
        block = ctx.enter_context(nc.Block())
        NL = 4 if shared else 2

        @block.sync
        def _(sp):
            sp.dma_start(wr[:, :], A[tag + "_wr"]).then_inc(w_loaded, 16)
            sp.dma_start(br[:, :], A[tag + "_br"].partition_broadcast(P)).then_inc(w_loaded, 16)
            if shared:
                sp.dma_start(ws[:, 0:2 * FF], A[tag + "_ws"]).then_inc(w_loaded, 16)
                sp.dma_start(ws[:, 2 * FF:], A[tag + "_wsd"]).then_inc(w_loaded, 16)
            for e in range(E):
                sp.dma_start(N.w[:, e, 0:WE], A[tag + "_w"][e]).then_inc(ew_loaded, 16)
                if N.width > WE:
                    sp.dma_start(N.w[:, e, WE:], A[tag + "_b2"][:, e * C:(e + 1) * C].partition_broadcast(P)).then_inc(ew_loaded, 16)
            sp.wait_ge(table_ready, 1)
            sp.wait_ge(consts, 5)
            for e in range(E):
                row = sp.value_load(tail[0:1, e:e + 1], min_val=e * REGION, max_val=e * REGION + B * S)
                sp.dma_start(N.rows_in[bass.ds(row, P), :], zeros[:, :]).then_inc(cleared, 16)
            sp.wait_ge(cleared, 16 * E)
            sp.wait_ge(ew_loaded, 16 * E * (2 if N.width > WE else 1))

        @block.gpsimd
        def _(pool):
            def chained(n, instruction):
                instruction.then_inc(consts, 1)
                pool.wait_ge(consts, n)

            chained(1, pool.memset(ones[:, :], 1.0))
            chained(2, pool.affine_select(out=earlier[:, :], in_=ones[:, :], compare_op=ALU.is_gt, fill=0.0,
                                          base=0, pattern=[[1, P]], channel_multiplier=-1))
            chained(3, pool.iota(e_i[:, :], pattern=[[1, E]], base=0, channel_multiplier=0))
            chained(4, pool.iota(slot_i[:, :], pattern=[[1, N.slots]], base=0, channel_multiplier=0))
            chained(5, pool.memset(zeros[:, :], 0.0))
            for c in range(CHUNKS):
                pool.wait_ge(routed, c + 1)
                pool.wait_ge(kept, (c + 1) * CG)
                for t in range(c * CT, (c + 1) * CT):
                    for k in range(K):
                        pool.indirect_dma_start(N.rows_in, bass.IndirectOffsetOnAxis(ap=N.pos_i[:, k, t:t + 1], axis=0),
                                                xn_all[:, t, :], None).then_inc(sent, 16)
            pool.wait_ge(sent, 16 * TILES * K)

        @block.scalar
        def _(act):
            def group(G, g):
                wait(act, xT_done, G + 1)
                act.activation(xnT[:, g, :], ps_x[:, 0:GT], ACT.Copy).then_inc(xT_ready, 1)
                wait(act, xn_ready, 2 * G + 2)
                act.activation(xn_all[:, bass.ds(2 * G, 2), :], xn[:, g, :, :], ACT.Copy).then_inc(kept, 1)
                if shared:
                    wait(act, ug_done, G + 1)
                    wait(act, h_ready, G)
                    act.activation(hg[:, :, :], ps_g[:, :, :], ACT.Silu).then_inc(g_ready, 1)

            for c in range(CHUNKS):
                def body(i):
                    for g in range(2):
                        group(2 * i + g, g)
                rounds(act, body, CG // 2 * (c + 1), first=(c == 0), last=0, start=CG // 2 * c)

        @block.vector
        def _(dve):
            links = [0]

            def step(*instructions):
                for x in instructions:
                    x.then_inc(link, 1)
                links[0] += len(instructions)
                dve.wait_ge(link, links[0])

            def over_tiles(t, n):
                return t.rearrange("p (a e) -> p a e", a=1).broadcast_to([P, n, E])

            def norm(G, g):
                wait(dve, xT_done, G - 1)
                wait(dve, kept, G - 1)
                for u in range(2):
                    dve.tensor_scalar(xn[:, g, u, :], R.x[:, 2 * G + u, :], R.mean[:, bass.ds(2 * G + u, 1)], R.rstd[:, bass.ds(2 * G + u, 1)],
                                      ALU.subtract, ALU.mult).then_inc(xn_ready, 1)
                if add_norm:
                    wait(dve, xn_ready, 2 * G + 2)
                    t = bass.ds(2 * G, 2)
                    dve.tensor_tensor(R.x[:, t, :], R.x[:, t, :], xn[:, g, :, :], ALU.add).then_inc(x_done, 1)

            def finish(G, g, t):
                wait(dve, l_done, G + 1)
                dve.tensor_tensor(logits[:, t, :], ps_l[:, 0:2 * E].rearrange("p (u e) -> p u e", u=2),
                                  br[:, :].rearrange("p (a e) -> p a e", a=1).broadcast_to([P, 2, E]), ALU.add).then_inc(l_ready, 1)
                if shared:
                    wait(dve, g_ready, G + 1)
                    dve.tensor_tensor(hT[:, g, :, :], ps_u[:, :, :], hg[:, :, :], ALU.mult).then_inc(h_ready, 1)
                    wait(dve, y_done, G + 1)
                    x = R.x[:, bass.ds(2 * G, 2), :]
                    dve.tensor_tensor(x, ps_y[:, 0:GT].rearrange("p (u c) -> p u c", u=2), x, ALU.add).then_inc(x_done, 1)

            dve.wait_ge(consts, 5)
            dve.wait_ge(w_loaded, 16 * NL)
            step(dve.tensor_copy(e_f[:, :], e_i[:, :]), dve.tensor_copy(slot_f[:, :], slot_i[:, :]))
            step(dve.tensor_scalar(start[:, :], e_f[:, :], float(REGION), None, ALU.mult))
            step(dve.tensor_copy(base[:, :], start[:, :]))
            for c in range(CHUNKS):
                def body(i):
                    for g in range(2):
                        norm(2 * i + g, g)
                    for g in range(2):
                        G = 2 * i + g
                        finish(G, g, bass.ds(2 * G - CT * c, 2))
                rounds(dve, body, CG // 2 * (c + 1), first=(c == 0), last=0, start=CG // 2 * c)
                wait(dve, l_ready, CG * (c + 1))
                tiles = slice(c * CT, (c + 1) * CT)
                step(*[dve.max(N.best[:, c * CT + t, :], logits[:, t, :]) for t in range(CT)])
                step(*[dve.max_index(index[:, t, :], N.best[:, c * CT + t, :], logits[:, t, :]) for t in range(CT)])
                step(dve.tensor_copy(index_f[:, :, :], index[:, :, 0:K]))
                step(*[dve.tensor_tensor(N.hit[:, k, tiles, :], over_tiles(e_f[:, :], CT),
                                         index_f[:, :, k:k + 1].broadcast_to([P, CT, E]), ALU.is_equal) for k in range(K)])
                if K == 2:
                    step(dve.tensor_tensor(chosen[:, :, :], N.hit[:, 0, tiles, :], N.hit[:, 1, tiles, :], ALU.add))
                else:
                    step(dve.tensor_copy(chosen[:, :, :], N.hit[:, 0, tiles, :]))
                dve.sem_inc(chosen_ready, 1)
                dve.wait_ge(ranked, c + 1)
                step(dve.tensor_tensor(rank[:, :, :], rank_ps[:, 0:CT, :], over_tiles(base[:, :], CT), ALU.add))
                step(dve.tensor_tensor(base[:, :], rank_ps[:, CT, :], base[:, :], ALU.add))
                for k in range(K):
                    step(dve.tensor_tensor(prod[:, 0:CT, :], N.hit[:, k, tiles, :], rank[:, :, :], ALU.mult))
                    step(dve.tensor_reduce(N.pos[:, k, tiles], prod[:, 0:CT, :], AX.X, ALU.add))
                    step(dve.tensor_copy(N.pos_i[:, k, tiles], N.pos[:, k, tiles]))
                dve.sem_inc(routed, 1)
            step(dve.tensor_copy(tail[:, :], base[:, :]), dve.tensor_tensor(need[:, :], base[:, :], start[:, :], ALU.subtract))
            step(dve.tensor_scalar(cnt_i[:, :], need[:, :], float(P - 1), None, ALU.add))
            step(dve.tensor_scalar(cnt_i[:, :], cnt_i[:, :], 7, None, ALU.arith_shift_right))
            step(dve.tensor_copy(need[:, :], cnt_i[:, :]))
            step(dve.tensor_copy(ends[:, :], need[:, :]))
            a, b, d = ends, ends2, 1
            while d < E:
                step(dve.tensor_copy(b[:, 0:d], a[:, 0:d]), dve.tensor_tensor(b[:, d:E], a[:, d:E], a[:, 0:E - d], ALU.add))
                a, b, d = b, a, 2 * d
            step(dve.tensor_tensor(need[:, :], a[:, :], need[:, :], ALU.subtract))
            step(dve.scalar_tensor_tensor(shift[:, :], need[:, :], float(P), start[:, :], ALU.mult, ALU.subtract))
            slots = lambda t: t.rearrange("p (a e) -> p a e", a=1).broadcast_to([P, N.slots, E])
            slot_b = lambda t: t.rearrange("p (s a) -> p s a", a=1).broadcast_to([P, N.slots, E])
            step(dve.tensor_tensor(by_slot[:, :, :], slots(a[:, :]), slot_b(slot_f[:, :]), ALU.is_le))
            step(dve.tensor_reduce(slot_x[:, :], by_slot[:, :, :], AX.X, ALU.add))
            step(dve.tensor_scalar(N.slot_e[:, :], slot_x[:, :], float(E - 1), None, ALU.min),
                 dve.tensor_tensor(by_slot[:, :, :], slots(e_f[:, :]), slot_b(slot_x[:, :]), ALU.is_equal))
            step(dve.tensor_tensor(by_slot[:, :, :], by_slot[:, :, :], slots(shift[:, :]), ALU.mult),
                 dve.tensor_scalar(slot_x[:, :], slot_x[:, :], float(E), None, ALU.is_lt))
            step(dve.tensor_scalar(slot_f[:, :], slot_f[:, :], float(P), None, ALU.mult))
            step(dve.tensor_tensor(slot_f[:, :], slot_f[:, :], slot_x[:, :], ALU.mult))
            step(dve.tensor_reduce(slot_x[:, :], by_slot[:, :, :], AX.X, ALU.add))
            step(dve.tensor_tensor(N.slot_row[:, :], slot_f[:, :], slot_x[:, :], ALU.subtract))
            dve.sem_inc(table_ready, 1)
            for k in range(K):
                step(dve.tensor_tensor(prod[:, :, :], N.hit[:, k, :, :], over_tiles(shift[:, :], TILES), ALU.mult))
                step(dve.tensor_reduce(moved[:, :], prod[:, :, :], AX.X, ALU.add))
                step(dve.tensor_tensor(N.pos[:, k, :], N.pos[:, k, :], moved[:, :], ALU.add))
            dve.wait_ge(sent, 16 * TILES * K)
            dve.tensor_copy(N.pos_i[:, :, :], N.pos[:, :, :]).then_inc(link, 1)

        @block.tensor
        def _(pe):
            def group(G, g):
                wait(pe, xn_ready, 2 * G + 2)
                wait(pe, xT_ready, G)
                for u in range(2):
                    last = pe.transpose(ps_x[:, u * P:(u + 1) * P], xn[:, g, u, :], R.ident[:, :])
                last.then_inc(xT_done, 1)
                wait(pe, xT_ready, G + 1)
                wait(pe, l_ready, G)
                for u in range(2):
                    last = pe.matmul(ps_l[:, u * E:(u + 1) * E], xnT[:, g, u * P:(u + 1) * P], wr[:, :], start=True, stop=True)
                last.then_inc(l_done, 1)
                if shared:
                    wait(pe, h_ready, G)
                    wait(pe, g_ready, G)
                    for out, at in ((ps_u, 0), (ps_g, FF)):
                        for j in range(HALVES):
                            last = pe.matmul(out[:, j, :], ws[:, at + j * P:at + (j + 1) * P], xnT[:, g, :], start=True, stop=True)
                    last.then_inc(ug_done, 1)
                    wait(pe, h_ready, G + 1)
                    wait(pe, x_done, G)
                    for u in range(2):
                        for j in range(HALVES):
                            last = pe.matmul(ps_y[:, u * P:(u + 1) * P], hT[:, g, j, u * P:(u + 1) * P],
                                             ws[:, 2 * FF + j * C:2 * FF + (j + 1) * C], start=(j == 0), stop=(j == HALVES - 1))
                    last.then_inc(y_done, 1)

            pe.wait_ge(w_loaded, 16 * NL)
            pe.wait_ge(consts, 5)
            for c in range(CHUNKS):
                def body(i):
                    for g in range(2):
                        group(2 * i + g, g)
                rounds(pe, body, CG // 2 * (c + 1), first=(c == 0), last=0, start=CG // 2 * c)
                pe.wait_ge(chosen_ready, c + 1)
                pe.matmul(rank_ps[:, 0:CT, :], earlier[:, :], chosen[:, :, :], start=True, stop=False, skip_group_check=True)
                for t in range(CT):
                    last = pe.matmul(rank_ps[:, t + 1:CT + 1, :], ones[:, :], chosen[:, t:t + 1, :].broadcast_to([P, CT - t, E]),
                                     start=False, stop=(t == CT - 1), skip_group_check=True)
                last.then_inc(ranked, 1)


def experts(nc, A, R, N, gated):
    tag, NS = N.tag, N.slots
    W = N.w.shape[2]
    H = 2 * FF if gated else FF
    B1 = H + HALVES * C
    B2 = B1 + HALVES
    with ExitStack() as ctx:
        sb = lambda name, shape, dt=F32: ctx.enter_context(nc.sbuf_tensor(f"{tag}e_{name}", shape, dt))
        ps = lambda name, shape: ctx.enter_context(nc.psum_tensor(f"{tag}e_{name}", shape, F32))
        sem = lambda name: R.semaphore(nc, f"{tag}e_{name}")
        NB = 4
        x = sb("x", [P, NB, C])
        xT = sb("xT", [P, 2, P])
        w = sb("w", [P, 2, W])
        hg = sb("hg", [P, HALVES, P])
        hT = sb("hT", [P, 2, HALVES, P])
        y = sb("y", [P, NB, C])
        ps_x, ps_y = [ps(f"ps_x{i}", [P, 512]) for i in range(2)], [ps(f"ps_y{i}", [P, 512]) for i in range(2)]
        ps_h = [ps(f"ps_h{i}", [P, H // P, P]) for i in range(2)]
        loaded = [sem(f"loaded{i}") for i in range(NB)]
        stored = [sem(f"stored{i}") for i in range(NB)]
        xT_done, xT_ready, w_ready = sem("xT_done"), sem("xT_ready"), sem("w_ready")
        passed, passed_sp = sem("passed"), sem("passed_sp")
        h_done, g_ready, h_ready, y_done, y_ready = (sem(n) for n in ("h_done", "g_ready", "h_ready", "y_done", "y_ready"))
        block = ctx.enter_context(nc.Block())

        @block.sync
        def _(sp):
            def body(i):
                for n in range(NB):
                    J = NB * i + n
                    wait(sp, xT_done, J - NB + 1)
                    settle(sp, passed_sp)
                    row = sp.value_load(N.slot_row[0:1, bass.ds(J, 1)], min_val=0, max_val=N.experts * N.REGION - P)
                    sp.dma_start(x[:, n, :], N.rows_in[bass.ds(row, P), :]).then_inc(loaded[n], 16)
            rounds(sp, body, NS // NB, last=0)

        @block.gpsimd
        def _(pool):
            def body(i):
                for n in range(NB):
                    J = NB * i + n
                    wait(pool, y_ready, J + 1)
                    pool.dma_start(N.rows_out[bass.ds(P * J, P), :], y[:, n, :]).then_inc(stored[n], 16)
            rounds(pool, body, NS // NB)
            for n in range(NB):
                pool.wait_ge(stored[n], 16 * (NS // NB))

        @block.vector
        def _(dve):
            def weights(J, m):
                wait(dve, y_done, J - 1)
                wait(dve, y_ready, J - 1)
                settle(dve, passed)
                e = dve.value_load(N.slot_e[0:1, bass.ds(J, 1)], min_val=0, max_val=N.experts - 1)
                dve.tensor_copy(w[:, m, :], N.w[:, bass.ds(e, 1), :].rearrange("p a c -> p (a c)")).then_inc(w_ready, 1)
                return e

            weights(0, 0)

            def body(i):
                for n in range(NB):
                    J, m = NB * i + n, n % 2
                    if within(J, NS):
                        wait(dve, xT_done, J + 1)
                        dve.tensor_copy(xT[:, m, :], ps_x[m][:, 0:P]).then_inc(xT_ready, 1)
                        if gated:
                            wait(dve, g_ready, J + 1)
                            dve.tensor_tensor(hT[:, m, :, :], ps_h[m][:, 0:HALVES, :], hg[:, :, :], ALU.mult).then_inc(h_ready, 1)
                    if within(J - 1, NS):
                        l = (n - 1) % NB
                        wait(dve, y_done, J)
                        wait(dve, stored[l], 16 * (i if n else i - 1))
                        if gated:
                            dve.tensor_copy(y[:, l, :], ps_y[1 - m][:, 0:C]).then_inc(y_ready, 1)
                        else:
                            dve.tensor_tensor(y[:, l, :], ps_y[1 - m][:, 0:C], w[:, 1 - m, B2:B2 + C], ALU.add).then_inc(y_ready, 1)
                    if within(J + 1, NS):
                        weights(J + 1, 1 - m)
            rounds(dve, body, NS // NB)
            body(NS // NB)

        @block.scalar
        def _(act):
            def body(i):
                for n in range(NB):
                    J, m = NB * i + n, n % 2
                    wait(act, h_done, J + 1)
                    if gated:
                        wait(act, h_ready, J)
                        act.activation(hg[:, :, :], ps_h[m][:, HALVES:2 * HALVES, :], ACT.Silu).then_inc(g_ready, 1)
                    else:
                        for j in range(HALVES):
                            last = act.activation(hT[:, m, j, :], ps_h[m][:, j, :], ACT.Gelu, bias=w[:, m, B1 + j:B1 + j + 1])
                        last.then_inc(h_ready, 1)
            rounds(act, body, NS // NB)

        @block.tensor
        def _(pe):
            def body(i):
                for n in range(NB):
                    J, m = NB * i + n, n % 2
                    if within(J, NS):
                        wait(pe, loaded[n], 16 * (i + 1))
                        wait(pe, xT_ready, J - 1)
                        pe.transpose(ps_x[m][:, 0:P], x[:, n, :], R.ident[:, :]).then_inc(xT_done, 1)
                        wait(pe, xT_ready, J + 1)
                        wait(pe, w_ready, J + 1)
                        wait(pe, h_ready, J - 1)
                        for j in range(H // P):
                            last = pe.matmul(ps_h[m][:, j, :], w[:, m, j * P:(j + 1) * P], xT[:, m, :], start=True, stop=True)
                        last.then_inc(h_done, 1)
                    if within(J - 1, NS):
                        wait(pe, h_ready, J)
                        wait(pe, y_ready, J - 2)
                        for j in range(HALVES):
                            last = pe.matmul(ps_y[1 - m][:, 0:C], hT[:, 1 - m, j, :], w[:, 1 - m, H + j * C:H + (j + 1) * C],
                                             start=(j == 0), stop=(j == HALVES - 1))
                        last.then_inc(y_done, 1)
            rounds(pe, body, NS // NB)
            body(NS // NB)


def combine(nc, R, N, out):
    tag, K = N.tag, N.top
    with ExitStack() as ctx:
        sb = lambda name, shape, dt=F32: ctx.enter_context(nc.sbuf_tensor(f"{tag}c_{name}", shape, dt))
        sem = lambda name: R.semaphore(nc, f"{tag}c_{name}")
        NB = 4
        got = sb("got", [P, NB, K, C])
        share = sb("share", [P, 2, TILES])
        arrived = [sem(f"arrived{n}") for n in range(NB)]
        link, e_ready, x_done, st_done, stored = sem("link"), sem("e_ready"), sem("x_done"), sem("st_done"), sem("stored")
        block = ctx.enter_context(nc.Block())

        @block.gpsimd
        def _(pool):
            for t in range(TILES):
                n = t % NB
                wait(pool, x_done, K * (t - NB + 1))
                for k in range(K):
                    pool.indirect_dma_start(got[:, n, k, :], None, N.rows_out,
                                            bass.IndirectOffsetOnAxis(ap=N.pos_i[:, k, t:t + 1], axis=0)).then_inc(arrived[n], 16)

        @block.scalar
        def _(act):
            if K == 2:
                act.wait_ge(link, 1)
                act.activation(share[:, 1, :], share[:, 1, :], ACT.Exp).then_inc(e_ready, 1)

        @block.vector
        def _(dve):
            if K == 2:
                dve.tensor_tensor(share[:, 1, :], N.best[:, :, 1], N.best[:, :, 0], ALU.subtract).then_inc(link, 1)
                dve.wait_ge(e_ready, 1)
                dve.tensor_scalar(share[:, 0, :], share[:, 1, :], 1.0, None, ALU.add).then_inc(link, 1)
                dve.wait_ge(link, 2)
                dve.reciprocal(share[:, 0, :], share[:, 0, :]).then_inc(link, 1)
                dve.wait_ge(link, 3)
                dve.tensor_tensor(share[:, 1, :], share[:, 1, :], share[:, 0, :], ALU.mult).then_inc(link, 1)
                dve.wait_ge(link, 4)

            def body(i):
                for n in range(NB):
                    t = NB * i + n
                    wait(dve, arrived[n], 16 * K * (i + 1))
                    for k in range(K):
                        if K == 2:
                            dve.scalar_tensor_tensor(R.x[:, t, :], got[:, n, k, :], share[:, k, bass.ds(t, 1)], R.x[:, t, :], ALU.mult, ALU.add).then_inc(x_done, 1)
                        else:
                            dve.tensor_tensor(R.x[:, t, :], got[:, n, k, :], R.x[:, t, :], ALU.add).then_inc(x_done, 1)
                        wait(dve, x_done, K * t + k + 1)
                    if out is None:
                        dve.bn_stats(R.stats[:, t, :], R.x[:, t, :]).then_inc(st_done, 1)
            rounds(dve, body, TILES // NB, first=0, last=0)

        if out is not None:
            @block.sync
            def _(sp):
                ST = 4
                for c in range(TILES // ST):
                    tiles = slice(c * ST, (c + 1) * ST)
                    sp.wait_ge(x_done, K * (c + 1) * ST)
                    sp.dma_start(out[:, tiles, :], R.x[:, tiles, :]).then_inc(stored, 16)
                sp.wait_ge(stored, 16 * (TILES // ST))


class Resident:

    def __init__(self, nc, ctx, A):
        sb = lambda name, shape, dt=F32: ctx.enter_context(nc.sbuf_tensor(name, shape, dt))
        self.semaphores = []
        self.x = sb("x_sb", [P, TILES, C])
        self.stats = sb("stats", [P, TILES, 6])
        self.mean, self.rstd = sb("mean", [P, TILES]), sb("rstd", [P, TILES])
        self.ident, self.ident16 = sb("ident", [P, P]), sb("ident16", [P, P], BF16)
        self.eps = sb("eps", [P, 1])
        self.xd = A["x"].rearrange("(t p) c -> p t c", p=P)

    def semaphore(self, nc, name):
        self.semaphores.append(nc.alloc_semaphore(name=name))
        return self.semaphores[-1]


def host_layout(I):
    import numpy as np

    t = lambda a: np.ascontiguousarray(np.asarray(a).T)
    r = lambda a, *s: np.ascontiguousarray(np.asarray(a)).reshape(*s)
    a = {
        "x": r(I["x"], B * S, C),
        "ctxT": t(r(I["ctx_1024"], B * S, C)),
        "pad": r(I["mask_BxS2_ik0"], 1, B * S),
        "a0_wq": t(I["L0_xattn_Wq"]), "a0_wk": t(I["L0_xattn_Wk"]), "a0_wo": t(I["L0_xattn_Wo"]),
        "a0_wv": r(t(I["L0_xattn_Wv"]).reshape(C, PAIRS, 2, D0).transpose(0, 2, 1, 3), C, C),
        "a0_bq": r(I["L0_xattn_bq"], C, 1), "a0_bk": r(I["L0_xattn_bk"], C, 1), "a0_bo": r(I["L0_xattn_bo"], 1, C),
        "a0_bv": r(np.asarray(I["L0_xattn_bv"]).reshape(PAIRS, 2, D0).transpose(1, 0, 2), 2, S),
        "mask": r(I["mask_BxSxS2_bf1"], B * S, S).view(np.uint8),
        "a1_wq": r(I["L1_xattn_Wq"], C, C), "a1_wo": r(I["L1_xattn_Wo"], C, C),
        "a1_wk": np.ascontiguousarray(np.asarray(I["L1_xattn_Wkv"])[:, :C]),
        "a1_wv": np.ascontiguousarray(np.asarray(I["L1_xattn_Wkv"])[:, C:]),
    }
    cat = lambda *xs: np.ascontiguousarray(np.concatenate(xs, axis=-1))
    halves = lambda w: np.asarray(w).reshape(*w.shape[:-2], HALVES, P, C)
    by_half = lambda w: np.moveaxis(halves(w), -3, -2).reshape(*w.shape[:-2], P, HALVES * C)
    turned = lambda w: np.swapaxes(np.asarray(w), -1, -2)
    a["f0_w"] = cat(I["L0_ffn_W1"], by_half(I["L0_ffn_W2"]), turned(np.asarray(I["L0_ffn_b1"]).reshape(E0, HALVES, P)))
    a["f0_b2"] = r(I["L0_ffn_b2"], 1, E0 * C)
    a["f0_wr"], a["f0_br"] = r(I["L0_ffn_Wr"], C, E0), r(I["L0_ffn_br"], 1, E0)
    a["f1_w"] = cat(turned(I["L1_ffn_up"]), turned(I["L1_ffn_gate"]), by_half(turned(I["L1_ffn_down"])))
    a["f1_wr"], a["f1_br"] = t(I["L1_ffn_router"]), np.zeros((1, E1), np.float32)
    a["f1_ws"] = cat(t(I["L1_ffn_w_up_s"]), t(I["L1_ffn_w_gate_s"]))
    a["f1_wsd"] = np.ascontiguousarray(by_half(t(I["L1_ffn_w_down_s"])))
    return a


def program(nc, A, out):
    tiled = out.rearrange("(t p) c -> p t c", p=P)
    with ExitStack() as ctx:
        R = Resident(nc, ctx, A)
        opening(nc, A, R)
        deviations(nc, R, "n0")
        layer0_attention(nc, A, R)
        end_phase(nc, R)
        deviations(nc, R, "n1")
        with ExitStack() as layer:
            N = Routing(nc, layer, "f0", E0, 2, FF + HALVES * C + HALVES + C)
            route(nc, A, R, N, add_norm=True, shared=False)
            experts(nc, A, R, N, gated=False)
            combine(nc, R, N, None)
        end_phase(nc, R)
        deviations(nc, R, "n2")
        layer1_attention(nc, A, R)
        end_phase(nc, R)
        deviations(nc, R, "n3")
        with ExitStack() as layer:
            N = Routing(nc, layer, "f1", E1, 1, 2 * FF + HALVES * C)
            route(nc, A, R, N, add_norm=False, shared=True)
            experts(nc, A, R, N, gated=True)
            combine(nc, R, N, tiled)
        end_phase(nc, R)


def kernel(**inputs):
    import concourse.bacc as bacc
    from concourse.bass_utils import run_bass_kernel_spmd

    nc = bacc.Bacc("TRN2", target_bir_lowering=False, num_devices=1)
    arrays = {"in_" + n: a for n, a in host_layout(inputs).items()}
    A = {n[3:]: nc.dram_tensor(n, a.shape, mybir.dt.from_np(a.dtype), kind="ExternalInput").ap() for n, a in arrays.items()}
    out = nc.dram_tensor("out", (B * S, C), F32, kind="ExternalOutput").ap()
    program(nc, A, out)
    result = run_bass_kernel_spmd(nc, [arrays], core_ids=[0]).results[0]["out"]
    return result.reshape(B, S, C)
```
